# Optimizing a Trainium2 kernel written in Bass

```python
import numpy as np
import jax
import jax.numpy as jnp

def _softmax(x, axis=-1):
    return jax.nn.softmax(x, axis=axis)

def _gelu(x):
    return jax.nn.gelu(x, approximate=True)

def _silu(x):
    return jax.nn.silu(x)

def _sigmoid(x):
    return jax.nn.sigmoid(x)

def _layernorm(x, axis=-1, eps=1e-05):
    m = jnp.mean(x, axis=axis, keepdims=True)
    v = jnp.var(x, axis=axis, keepdims=True)
    return (x - m) / jnp.sqrt(v + eps)

def _scatter_add(tgt, idx, src, axis=0):
    return tgt.at[idx].add(src)

def _segment_sum(src, seg, n):
    return jax.ops.segment_sum(src, seg, n)
kernel_name = 'mk_dlrm_tower_d1_rec_r8_28b0a1'

def setup_inputs(seed: int=0):
    np.random.seed(seed)
    _w = jnp.asarray

    def _rec_inputs():
        import jax
        import jax.numpy as jnp
        _tk = jax.random.key(seed)
        dense_ctx = jax.random.normal(jax.random.fold_in(_tk, 190), (1024, 16), jnp.float32)
        ids = jnp.stack([jax.random.randint(jax.random.fold_in(_tk, 200 + f), (1024,), 0, v, jnp.int32) for f, v in enumerate([125000, 125000, 125000, 12500, 12500, 1250, 12500, 12500, 125000, 1000, 1000, 1000, 125000, 12500, 12500, 1000, 125000, 125000, 12500, 1250, 12500, 12500, 125000, 1250, 1250, 12500, 1000, 125000, 12500, 125000, 1000, 12500, 125000, 12500, 1000, 1250, 12500, 1000, 1250])], axis=1)
        tbl_0 = 0.05 * jax.random.normal(jax.random.fold_in(_tk, 500 + 0), (125000, 16), jnp.float32)
        tbl_1 = 0.05 * jax.random.normal(jax.random.fold_in(_tk, 500 + 1), (125000, 16), jnp.float32)
        tbl_2 = 0.05 * jax.random.normal(jax.random.fold_in(_tk, 500 + 2), (125000, 16), jnp.float32)
        tbl_3 = 0.05 * jax.random.normal(jax.random.fold_in(_tk, 500 + 3), (12500, 16), jnp.float32)
        tbl_4 = 0.05 * jax.random.normal(jax.random.fold_in(_tk, 500 + 4), (12500, 16), jnp.float32)
        tbl_5 = 0.05 * jax.random.normal(jax.random.fold_in(_tk, 500 + 5), (1250, 16), jnp.float32)
        tbl_6 = 0.05 * jax.random.normal(jax.random.fold_in(_tk, 500 + 6), (12500, 16), jnp.float32)
        tbl_7 = 0.05 * jax.random.normal(jax.random.fold_in(_tk, 500 + 7), (12500, 16), jnp.float32)
        tbl_8 = 0.05 * jax.random.normal(jax.random.fold_in(_tk, 500 + 8), (125000, 16), jnp.float32)
        tbl_9 = 0.05 * jax.random.normal(jax.random.fold_in(_tk, 500 + 9), (1000, 16), jnp.float32)
        tbl_10 = 0.05 * jax.random.normal(jax.random.fold_in(_tk, 500 + 10), (1000, 16), jnp.float32)
        tbl_11 = 0.05 * jax.random.normal(jax.random.fold_in(_tk, 500 + 11), (1000, 16), jnp.float32)
        tbl_12 = 0.05 * jax.random.normal(jax.random.fold_in(_tk, 500 + 12), (125000, 16), jnp.float32)
        tbl_13 = 0.05 * jax.random.normal(jax.random.fold_in(_tk, 500 + 13), (12500, 16), jnp.float32)
        tbl_14 = 0.05 * jax.random.normal(jax.random.fold_in(_tk, 500 + 14), (12500, 16), jnp.float32)
        tbl_15 = 0.05 * jax.random.normal(jax.random.fold_in(_tk, 500 + 15), (1000, 16), jnp.float32)
        tbl_16 = 0.05 * jax.random.normal(jax.random.fold_in(_tk, 500 + 16), (125000, 16), jnp.float32)
        tbl_17 = 0.05 * jax.random.normal(jax.random.fold_in(_tk, 500 + 17), (125000, 16), jnp.float32)
        tbl_18 = 0.05 * jax.random.normal(jax.random.fold_in(_tk, 500 + 18), (12500, 16), jnp.float32)
        tbl_19 = 0.05 * jax.random.normal(jax.random.fold_in(_tk, 500 + 19), (1250, 16), jnp.float32)
        tbl_20 = 0.05 * jax.random.normal(jax.random.fold_in(_tk, 500 + 20), (12500, 16), jnp.float32)
        tbl_21 = 0.05 * jax.random.normal(jax.random.fold_in(_tk, 500 + 21), (12500, 16), jnp.float32)
        tbl_22 = 0.05 * jax.random.normal(jax.random.fold_in(_tk, 500 + 22), (125000, 16), jnp.float32)
        tbl_23 = 0.05 * jax.random.normal(jax.random.fold_in(_tk, 500 + 23), (1250, 16), jnp.float32)
        tbl_24 = 0.05 * jax.random.normal(jax.random.fold_in(_tk, 500 + 24), (1250, 16), jnp.float32)
        tbl_25 = 0.05 * jax.random.normal(jax.random.fold_in(_tk, 500 + 25), (12500, 16), jnp.float32)
        tbl_26 = 0.05 * jax.random.normal(jax.random.fold_in(_tk, 500 + 26), (1000, 16), jnp.float32)
        tbl_27 = 0.05 * jax.random.normal(jax.random.fold_in(_tk, 500 + 27), (125000, 16), jnp.float32)
        tbl_28 = 0.05 * jax.random.normal(jax.random.fold_in(_tk, 500 + 28), (12500, 16), jnp.float32)
        tbl_29 = 0.05 * jax.random.normal(jax.random.fold_in(_tk, 500 + 29), (125000, 16), jnp.float32)
        tbl_30 = 0.05 * jax.random.normal(jax.random.fold_in(_tk, 500 + 30), (1000, 16), jnp.float32)
        tbl_31 = 0.05 * jax.random.normal(jax.random.fold_in(_tk, 500 + 31), (12500, 16), jnp.float32)
        tbl_32 = 0.05 * jax.random.normal(jax.random.fold_in(_tk, 500 + 32), (125000, 16), jnp.float32)
        tbl_33 = 0.05 * jax.random.normal(jax.random.fold_in(_tk, 500 + 33), (12500, 16), jnp.float32)
        tbl_34 = 0.05 * jax.random.normal(jax.random.fold_in(_tk, 500 + 34), (1000, 16), jnp.float32)
        tbl_35 = 0.05 * jax.random.normal(jax.random.fold_in(_tk, 500 + 35), (1250, 16), jnp.float32)
        tbl_36 = 0.05 * jax.random.normal(jax.random.fold_in(_tk, 500 + 36), (12500, 16), jnp.float32)
        tbl_37 = 0.05 * jax.random.normal(jax.random.fold_in(_tk, 500 + 37), (1000, 16), jnp.float32)
        tbl_38 = 0.05 * jax.random.normal(jax.random.fold_in(_tk, 500 + 38), (1250, 16), jnp.float32)
        _rk = jax.random.fold_in(_tk, 7)
        W_top1 = 0.0693375 * jax.random.normal(jax.random.fold_in(_tk, 801), (208, 512), jnp.float32)
        W_top2 = 0.0441942 * jax.random.normal(jax.random.fold_in(_tk, 802), (512, 256), jnp.float32)
        W_top3 = 0.0625 * jax.random.normal(jax.random.fold_in(_tk, 803), (256, 1), jnp.float32)
        b_top1 = jnp.zeros((512,), jnp.float32)
        b_top2 = jnp.zeros((256,), jnp.float32)
        return (dense_ctx, ids, tbl_0, tbl_1, tbl_2, tbl_3, tbl_4, tbl_5, tbl_6, tbl_7, tbl_8, tbl_9, tbl_10, tbl_11, tbl_12, tbl_13, tbl_14, tbl_15, tbl_16, tbl_17, tbl_18, tbl_19, tbl_20, tbl_21, tbl_22, tbl_23, tbl_24, tbl_25, tbl_26, tbl_27, tbl_28, tbl_29, tbl_30, tbl_31, tbl_32, tbl_33, tbl_34, tbl_35, tbl_36, tbl_37, tbl_38, W_top1, b_top1, W_top2, b_top2, W_top3)
    dense_ctx, ids, tbl_0, tbl_1, tbl_2, tbl_3, tbl_4, tbl_5, tbl_6, tbl_7, tbl_8, tbl_9, tbl_10, tbl_11, tbl_12, tbl_13, tbl_14, tbl_15, tbl_16, tbl_17, tbl_18, tbl_19, tbl_20, tbl_21, tbl_22, tbl_23, tbl_24, tbl_25, tbl_26, tbl_27, tbl_28, tbl_29, tbl_30, tbl_31, tbl_32, tbl_33, tbl_34, tbl_35, tbl_36, tbl_37, tbl_38, W_top1, b_top1, W_top2, b_top2, W_top3 = _rec_inputs()

    def _L0_rec_setup():
        import jax, jax.numpy as jnp
        import numpy as np
        key = jax.random.key(seed)
        k1, k2, k3 = jax.random.split(key, 3)
        B, F0, D = (1024, 39, 16)
        L = 128
        hash_x = jax.random.normal(k1, (B, F0, D), dtype=jnp.float32)
        W0 = jax.random.normal(k2, (F0 * F0, L), dtype=jnp.float32) * 0.05
        W1 = jax.random.normal(k3, (F0 * (L // 2), L), dtype=jnp.float32) * 0.05
        return {'hash_x': hash_x, 'W0': W0, 'W1': W1}
    _L0_rec_all = _L0_rec_setup()
    _L0_rec_in = {k: v for k, v in _L0_rec_all.items() if k in ('W0', 'W1')}
    del _L0_rec_all
    return {'dense_ctx': dense_ctx, 'ids': ids, 'tbl_0': tbl_0, 'tbl_1': tbl_1, 'tbl_2': tbl_2, 'tbl_3': tbl_3, 'tbl_4': tbl_4, 'tbl_5': tbl_5, 'tbl_6': tbl_6, 'tbl_7': tbl_7, 'tbl_8': tbl_8, 'tbl_9': tbl_9, 'tbl_10': tbl_10, 'tbl_11': tbl_11, 'tbl_12': tbl_12, 'tbl_13': tbl_13, 'tbl_14': tbl_14, 'tbl_15': tbl_15, 'tbl_16': tbl_16, 'tbl_17': tbl_17, 'tbl_18': tbl_18, 'tbl_19': tbl_19, 'tbl_20': tbl_20, 'tbl_21': tbl_21, 'tbl_22': tbl_22, 'tbl_23': tbl_23, 'tbl_24': tbl_24, 'tbl_25': tbl_25, 'tbl_26': tbl_26, 'tbl_27': tbl_27, 'tbl_28': tbl_28, 'tbl_29': tbl_29, 'tbl_30': tbl_30, 'tbl_31': tbl_31, 'tbl_32': tbl_32, 'tbl_33': tbl_33, 'tbl_34': tbl_34, 'tbl_35': tbl_35, 'tbl_36': tbl_36, 'tbl_37': tbl_37, 'tbl_38': tbl_38, 'W_top1': W_top1, 'b_top1': b_top1, 'W_top2': W_top2, 'b_top2': b_top2, 'W_top3': W_top3, 'L0_rec_W0': _L0_rec_in['W0'], 'L0_rec_W1': _L0_rec_in['W1']}

def reference(dense_ctx, ids, tbl_0, tbl_1, tbl_2, tbl_3, tbl_4, tbl_5, tbl_6, tbl_7, tbl_8, tbl_9, tbl_10, tbl_11, tbl_12, tbl_13, tbl_14, tbl_15, tbl_16, tbl_17, tbl_18, tbl_19, tbl_20, tbl_21, tbl_22, tbl_23, tbl_24, tbl_25, tbl_26, tbl_27, tbl_28, tbl_29, tbl_30, tbl_31, tbl_32, tbl_33, tbl_34, tbl_35, tbl_36, tbl_37, tbl_38, W_top1, b_top1, W_top2, b_top2, W_top3, L0_rec_W0, L0_rec_W1):
    import jax
    import jax.numpy as jnp

    def _L0_rec_ref(hash_x, W0, W1):
        import jax, jax.numpy as jnp
        import numpy as np
        x0 = hash_x
        B, F0, D = x0.shape
        L = W0.shape[1]
        z0 = jnp.einsum('bid,bjd->bdij', x0, x0).reshape(B, D, F0 * F0)
        cur0 = jax.nn.relu(jnp.einsum('bdk,kl->bld', z0, W0))
        next_h, direct0 = jnp.split(cur0, 2, axis=1)
        Fk = next_h.shape[1]
        z1 = jnp.einsum('bid,bjd->bdij', x0, next_h).reshape(B, D, F0 * Fk)
        cur1 = jax.nn.relu(jnp.einsum('bdk,kl->bld', z1, W1))
        result = jnp.concatenate([direct0, cur1], axis=1)
        return jnp.sum(result, axis=-1)
    e = jnp.stack([tbl_0[ids[:, 0]], tbl_1[ids[:, 1]], tbl_2[ids[:, 2]], tbl_3[ids[:, 3]], tbl_4[ids[:, 4]], tbl_5[ids[:, 5]], tbl_6[ids[:, 6]], tbl_7[ids[:, 7]], tbl_8[ids[:, 8]], tbl_9[ids[:, 9]], tbl_10[ids[:, 10]], tbl_11[ids[:, 11]], tbl_12[ids[:, 12]], tbl_13[ids[:, 13]], tbl_14[ids[:, 14]], tbl_15[ids[:, 15]], tbl_16[ids[:, 16]], tbl_17[ids[:, 17]], tbl_18[ids[:, 18]], tbl_19[ids[:, 19]], tbl_20[ids[:, 20]], tbl_21[ids[:, 21]], tbl_22[ids[:, 22]], tbl_23[ids[:, 23]], tbl_24[ids[:, 24]], tbl_25[ids[:, 25]], tbl_26[ids[:, 26]], tbl_27[ids[:, 27]], tbl_28[ids[:, 28]], tbl_29[ids[:, 29]], tbl_30[ids[:, 30]], tbl_31[ids[:, 31]], tbl_32[ids[:, 32]], tbl_33[ids[:, 33]], tbl_34[ids[:, 34]], tbl_35[ids[:, 35]], tbl_36[ids[:, 36]], tbl_37[ids[:, 37]], tbl_38[ids[:, 38]]], axis=1)
    z = _L0_rec_ref(e, L0_rec_W0, L0_rec_W1)
    z = z.reshape(z.shape[0], -1)
    h = jnp.concatenate([z, dense_ctx], axis=1)
    h = jnp.maximum(h @ W_top1 + b_top1, 0.0)
    h = jnp.maximum(h @ W_top2 + b_top2, 0.0)
    y = h @ W_top3
    return y

_drawn_inputs = setup_inputs


def setup_inputs(seed=0):
    import zlib

    import numpy as np

    out = dict(_drawn_inputs(seed))
    spreads = {'b_top1': (0.0, 0.8), 'b_top2': (0.0, 0.437)}
    factors = {'tbl_0': 8.0,
     'tbl_1': 8.0,
     'tbl_2': 8.0,
     'tbl_3': 8.0,
     'tbl_4': 8.0,
     'tbl_5': 8.0,
     'tbl_6': 8.0,
     'tbl_7': 8.0,
     'tbl_8': 8.0,
     'tbl_9': 8.0,
     'tbl_10': 8.0,
     'tbl_11': 8.0,
     'tbl_12': 8.0,
     'tbl_13': 8.0,
     'tbl_14': 8.0,
     'tbl_15': 8.0,
     'tbl_16': 8.0,
     'tbl_17': 8.0,
     'tbl_18': 8.0,
     'tbl_19': 8.0,
     'tbl_20': 8.0,
     'tbl_21': 8.0,
     'tbl_22': 8.0,
     'tbl_23': 8.0,
     'tbl_24': 8.0,
     'tbl_25': 8.0,
     'tbl_26': 8.0,
     'tbl_27': 8.0,
     'tbl_28': 8.0,
     'tbl_29': 8.0,
     'tbl_30': 8.0,
     'tbl_31': 8.0,
     'tbl_32': 8.0,
     'tbl_33': 8.0,
     'tbl_34': 8.0,
     'tbl_35': 8.0,
     'tbl_36': 8.0,
     'tbl_37': 8.0,
     'tbl_38': 8.0,
     'L0_rec_W1': 8.0}
    for name, (base, spread) in spreads.items():
        noise = np.random.default_rng([zlib.crc32(name.encode()), seed]).standard_normal(out[name].shape)
        drawn = base * np.exp(spread * noise) if base else spread * noise
        out[name] = jnp.asarray(drawn.astype(out[name].dtype))
    for name, factor in factors.items():
        out[name] = (out[name] * factor).astype(out[name].dtype)
    return out
```

```python
from contextlib import ExitStack

import numpy as np

import concourse.bass as bass
from concourse import mybir

F32 = mybir.dt.float32
F32R = mybir.dt.float32r
BF16 = mybir.dt.bfloat16
I32 = mybir.dt.int32
ALU = mybir.AluOpType
ACT = mybir.ActivationFunctionType
AX = mybir.AxisListType

P = 128
B, FIELDS, D = 1024, 39, 16
L = 128
HID = L // 2
DENSE, H1, H2 = 16, 512, 256
GROUPS = B // P
DT = D // 2
TILE = DT * P
BANK = 512
TILES = 2 * GROUPS
SHIFTS = FIELDS // 2 + 1
PER0 = P // FIELDS
C0 = -(-SHIFTS // PER0)
C1 = -(-FIELDS // 2)
K0 = PER0 * FIELDS
BLOCK = C0 + C1
CHUNKS = TILES * BLOCK
BODY = 2 * BLOCK
FIRST = C0 + BLOCK
BODIES = GROUPS - 1
LAST = FIRST + (BODIES - 1) * BODY
TAIL = FIRST + BODIES * BODY
NBUF = 6

LOW = ["p" if q % 2 else "v" for q in range(BLOCK)]
REP_AHEAD, PROD_AHEAD, HIGH_AHEAD, LOW_AHEAD = 5, 4, 3, 3
Q_HID, Q_SPLIT, Q_SUM, Q_COPIES, Q_TURN, Q_KEEP = C0 - 1, 0, 3, 10, 14, 22
Q_GATHER = next(q for q in range(C0 - 1, 0, -1) if LOW[q + LOW_AHEAD] == "p")
GATHER_CUT = 20


def rows0(c):
    return FIELDS * (min(SHIFTS, PER0 * c + PER0) - PER0 * c)


def place(n):
    k, q = (0, n) if n < C0 else (1 + (n - C0) // BLOCK, (n - C0) % BLOCK)
    if n >= TAIL:
        k, q = 2 * BODIES + 2, n - TAIL + C0
    return (k, 0, q, q) if q < C0 else (k, 1, q - C0, q)


def counts(wanted):
    out = [0]
    for n in range(CHUNKS):
        out.append(out[-1] + wanted(LOW[place(n)[3]]))
    return out


BEFORE = {who: counts(lambda w, who=who: w == who) for who in "vp"}
BEFORE["high"] = counts(lambda w: w != "-")


def through(what, n, T):
    before = BEFORE[what]
    return before[n + 1] + (before[FIRST + BODY] - before[FIRST]) * T


def program(nc, dense_t, ids, tables, w0_a, w0_b, w1, sel0, sel1, eye16, eye32,
            wt1, bt1, wt2, bt2, wt3, y):
    with ExitStack() as ctx:
        def sb(name, shape, dt):
            return ctx.enter_context(nc.sbuf_tensor(name, shape, dt))

        def psum(name, shape, dt):
            return ctx.enter_context(nc.psum_tensor(name, shape, dt))

        def sem(name):
            return ctx.enter_context(nc.semaphore(name))

        w0_sb, w0_t = sb("w0_sb", [K0, C0, L], F32), sb("w0_t", [K0, C0, L], F32)
        w0_high, w0_low = sb("w0_high", [K0, C0, L], F32R), sb("w0_low", [K0, C0, L], F32R)
        w1_sb = sb("w1_sb", [P, C1, L], F32)
        w1_high, w1_low = sb("w1_high", [P, C1, L], F32R), sb("w1_low", [P, C1, L], F32R)
        sel0_sb, sel1_sb = sb("sel0_sb", [K0, C0, P], BF16), sb("sel1_sb", [K0, C1, P], BF16)
        eye16_sb, eye32_sb = sb("eye16_sb", [P, P], BF16), sb("eye32_sb", [P, P], F32)
        wt1_cur, wt1_dir = sb("wt1_cur", [L, H1], F32), sb("wt1_dir", [HID + DENSE, H1], F32)
        wt2_sb, wt3_sb = sb("wt2_sb", [P, H1 // P, H2], F32), sb("wt3_sb", [P, H2 // P], F32)
        bt1_sb, bt2_sb = sb("bt1_sb", [P, H1 // P], F32), sb("bt2_sb", [P, H2 // P], F32)

        ids_sb = sb("ids_sb", [P, FIELDS], I32)
        gathered = sb("gathered", [P, FIELDS, D], F32)
        copies_b = sb("copies_b", [P, D, PER0, FIELDS], F32)
        parts_b = sb("parts_b", [P, D, 3, FIELDS], BF16)
        rest_b = sb("rest_b", [P, D, FIELDS], F32)

        x_copies = sb("x_copies", [K0, 2, TILE], F32)
        x_parts = sb("x_parts", [K0, 2, TILE], BF16)
        hidden = sb("hidden", [P, 2, TILE], F32)

        z = sb("z", [P, NBUF, TILE], F32)
        z_high, z_low = sb("z_high", [P, NBUF, TILE], F32R), sb("z_low", [P, NBUF, TILE], F32R)

        direct0, cur1 = sb("direct0", [HID, 2, TILE], F32), sb("cur1", [P, 2, TILE], F32)
        top_dir, top_cur = sb("top_dir", [HID + DENSE, B], F32), sb("top_cur", [P, B], F32)
        mlp1, mlp2 = z[:, 0:H1 // P, :], z[:, H1 // P:H1 // P + H2 // P, :]
        y_sb = sb("y_sb", [1, B], F32)

        acc0, acc1 = psum("acc0", [P, TILE], F32), psum("acc1", [P, TILE], F32)
        rep = psum("rep", [P, 2, TILE], F32)

        weights_in, sel_in, eye_in, top_in = sem("weights_in"), sem("sel_in"), sem("eye_in"), sem("top_in")
        w_summed, w_high_done, w_low_done = sem("w_summed"), sem("w_high_done"), sem("w_low_done")
        ids_in, rows_in = sem("ids_in"), sem("rows_in")
        split_step = sem("split_step")
        parts_ready, copies_ready = sem("parts_ready"), sem("copies_ready")
        parts_turned, copies_turned = sem("parts_turned"), sem("copies_turned")
        parts_kept, copies_kept = sem("parts_kept"), sem("copies_kept")
        rep_done, prod_done, main_done = sem("rep_done"), sem("prod_done"), sem("main_done")
        high_done, low_v_done, low_p_done = sem("high_done"), sem("low_v_done"), sem("low_p_done")
        hid_done, cur1_done = sem("hid_done"), sem("cur1_done")
        direct_summed, cur_summed = sem("direct_summed"), sem("cur_summed")
        mlp_mm, mlp_act, mlp_vec, y_out = sem("mlp_mm"), sem("mlp_act"), sem("mlp_vec"), sem("y_out")

        block = ctx.enter_context(nc.Block())

        def turned_to(k_tile, of):
            if of == "copies":
                return acc1 if k_tile == 1 else acc0
            to = rep[:, k_tile, 0:BANK] if k_tile < 2 else acc0[:, 0:BANK]
            return to.bitcast(BF16)

        @block.sync
        def _(sp):
            sp.dma_start(ids_sb[:, :], ids[0, :, :]).then_inc(ids_in, 16)
            for dst, src in ((w0_sb, w0_a), (w0_t, w0_b), (w1_sb, w1)):
                sp.dma_start(dst[:, :, :], src).then_inc(weights_in, 16)
            for dst, src in ((eye16_sb, eye16), (eye32_sb, eye32)):
                sp.dma_start(dst[:, :], src).then_inc(eye_in, 16)
            for dst, src in ((sel0_sb, sel0), (sel1_sb, sel1)):
                sp.dma_start(dst[:, :, :], src).then_inc(sel_in, 16)
            for dst, src in ((top_dir[HID:, :], dense_t), (wt1_cur[:, :], wt1[HID:HID + L, :]),
                             (wt1_dir[0:HID, :], wt1[0:HID, :]), (wt1_dir[HID:, :], wt1[HID + L:, :]),
                             (wt2_sb[:, :, :], wt2), (wt3_sb[:, :], wt3),
                             (bt1_sb[:, :], bt1), (bt2_sb[:, :], bt2)):
                sp.dma_start(dst, src).then_inc(top_in, 16)
            with sp.Fori(1, GROUPS) as j:
                sp.wait_ge(rows_in, j * (16 * FIELDS))
                sp.dma_start(ids_sb[:, :], ids[bass.ds(j, 1), :, :].rearrange("j p f -> (j p) f"))\
                  .then_inc(ids_in, 16)
            for h in range(2):
                sp.wait_ge(mlp_act, 6 + h + 1)
                sp.dma_start(y[:, h * BANK:(h + 1) * BANK], y_sb[:, h * BANK:(h + 1) * BANK])\
                  .then_inc(y_out, 16)
            sp.wait_ge(y_out, 32)

        @block.gpsimd
        def _(pool):
            def gather(f):
                pool.indirect_dma_start(
                    out=gathered[:, f, :], out_offset=None, in_=tables[f],
                    in_offset=bass.IndirectOffsetOnAxis(ap=ids_sb[:, f:f + 1], axis=0)).then_inc(rows_in, 16)

            def low(n, T):
                pool.wait_ge(high_done, through("high", n, T))
                if n >= NBUF:
                    pool.wait_ge(main_done, n - NBUF + 1 + BODY * T)
                k, layer, c, q = place(n)
                rows, buf = (P if layer else rows0(c)), n % NBUF
                pool.tensor_tensor(z_low[0:rows, buf, :], z[0:rows, buf, :],
                                   z_high[0:rows, buf, :].bitcast(F32), ALU.subtract).then_inc(low_p_done, 1)

            def step(n, T=0):
                k, layer, c, q = place(n)
                group = (k + 3) // 2 if k % 2 else (k + 2) // 2
                if k % 2 and q == Q_GATHER and group < GROUPS:
                    pool.wait_ge(parts_ready, group + T)
                    pool.wait_ge(copies_ready, group + T)
                    pool.wait_ge(ids_in, 16 * (group + 1) + 16 * T)
                if n + LOW_AHEAD < CHUNKS and LOW[place(n + LOW_AHEAD)[3]] == "p":
                    low(n + LOW_AHEAD, T)
                if k >= 1 and group < GROUPS:
                    if k % 2 and q >= C0:
                        f = q - C0
                        gather(f)
                    elif k % 2 == 0 and GATHER_CUT + q < FIELDS:
                        gather(GATHER_CUT + q)

            pool.wait_ge(ids_in, 16)
            for f in range(FIELDS):
                gather(f)
            pool.wait_ge(parts_ready, 1)
            pool.wait_ge(copies_ready, 1)
            pool.wait_ge(ids_in, 32)
            for f in range(FIELDS):
                gather(f)
            for n in range(LOW_AHEAD):
                if LOW[place(n)[3]] == "p":
                    low(n, 0)
            for n in range(FIRST):
                step(n)
            with pool.Fori(0, BODIES - 2) as T:
                for n in range(FIRST, FIRST + BODY):
                    step(n, T)
            for n in range(LAST - BODY, CHUNKS):
                step(n)

        @block.scalar
        def _(act):
            def copies(j, T=0):
                act.wait_ge(rows_in, 16 * FIELDS * (j + 1) + 16 * FIELDS * T)
                if j >= 1:
                    act.wait_ge(copies_turned, 2 * j + 2 * T)
                nc.scalar.activation(copies_b[:, :, :, :],
                                     gathered[:, :, :].rearrange("p f d -> p d f").unsqueeze(2)
                                     .broadcast_to([P, D, PER0, FIELDS]), ACT.Copy).then_inc(copies_ready, 1)

            def keep_copies(k_tile, T=0):
                act.wait_ge(copies_turned, k_tile + 1 + 2 * T)
                nc.scalar.activation(x_copies[:, k_tile % 2, :], turned_to(k_tile, "copies")[0:K0, :],
                                     ACT.Copy).then_inc(copies_kept, 1)

            def keep_parts(k_tile, T=0):
                act.wait_ge(parts_turned, k_tile + 1 + 2 * T)
                nc.scalar.activation(x_parts[:, k_tile % 2, :], turned_to(k_tile, "parts")[0:K0, :],
                                     ACT.Copy).then_inc(parts_kept, 1)

            def high(n, T=0):
                k, layer, c, q = place(n)
                if LOW[q] == "-":
                    return
                act.wait_ge(prod_done, n + 1 + BODY * T)
                if n >= NBUF:
                    act.wait_ge(main_done, n - NBUF + 1 + BODY * T)
                rows, buf = (P if layer else rows0(c)), n % NBUF
                nc.scalar.activation(z_high[0:rows, buf, :], z[0:rows, buf, :], ACT.Copy).then_inc(high_done, 1)

            def keep_layer0(k, n, T):
                act.wait_ge(main_done, n + 1 + BODY * T)
                if k >= 2:
                    act.wait_ge(prod_done, n - Q_HID + BODY * T)
                if k >= 2 and k % 2 == 0:
                    act.wait_ge(direct_summed, k // 2 + T)
                half = k % 2
                nc.scalar.activation(hidden[0:HID, half, :], acc0[0:HID, :], ACT.Relu)
                nc.scalar.activation(hidden[HID:P, half, :], acc0[0:HID, :], ACT.Relu)
                nc.scalar.activation(direct0[:, half, :], acc0[HID:P, :], ACT.Relu).then_inc(hid_done, 1)

            def keep_layer1(k, n, T):
                act.wait_ge(main_done, n + 1 + BODY * T)
                if k >= 3 and (k - 1) % 2 == 0:
                    act.wait_ge(cur_summed, (k - 1) // 2 + T)
                nc.scalar.activation(cur1[:, (k - 1) % 2, :], acc1[:, :], ACT.Relu).then_inc(cur1_done, 1)

            def step(n, T=0):
                k, layer, c, q = place(n)
                if n + HIGH_AHEAD < CHUNKS:
                    high(n + HIGH_AHEAD, T)
                if layer == 0 and q == Q_HID:
                    keep_layer0(k, n, T)
                if k % 2 and q == Q_SPLIT and (k + 1) // 2 < GROUPS:
                    copies((k + 1) // 2, T)
                if 1 <= k < TILES - 1:
                    if q == Q_COPIES:
                        keep_copies(k + 1, T)
                    if q == Q_KEEP:
                        act.wait_ge(rep_done, n - q + BLOCK + BODY * T)
                        keep_parts(k + 1, T)
                if q == BLOCK - 1:
                    keep_layer1(k, n, T)

            act.wait_ge(w_summed, 1)
            nc.scalar.activation(w0_high[:, :, :], w0_sb[:, :, :], ACT.Copy).then_inc(w_high_done, 1)
            act.wait_ge(weights_in, 48)
            nc.scalar.activation(w1_high[:, :, :], w1_sb[:, :, :], ACT.Copy).then_inc(w_high_done, 1)
            copies(0)
            for k_tile in range(2):
                keep_copies(k_tile)
                keep_parts(k_tile)
            for n in range(HIGH_AHEAD):
                high(n)
            for n in range(FIRST):
                step(n)
            with act.Fori(0, BODIES - 1) as T:
                for n in range(FIRST, FIRST + BODY):
                    step(n, T)
            for n in range(LAST, CHUNKS):
                step(n)

            act.wait_ge(top_in, 128)
            for h in range(2):
                cols = slice(h * BANK, (h + 1) * BANK)
                for m in (0, 2):
                    act.wait_ge(mlp_mm, 4 * h + m + 1)
                    src = (acc0, acc1)[m // 2][:, 0:BANK] if h == 0 else rep[:, m // 2, 0:BANK]
                    nc.scalar.activation(mlp1[:, m, cols], src, ACT.Relu, bias=bt1_sb[:, m:m + 1])\
                      .then_inc(mlp_act, 1)
            for h in range(2):
                cols = slice(h * BANK, (h + 1) * BANK)
                act.wait_ge(mlp_mm, 8 + 2 * h + 1)
                nc.scalar.activation(mlp2[:, 0, cols], (acc0, acc1)[h][:, 0:BANK], ACT.Relu,
                                     bias=bt2_sb[:, 0:1]).then_inc(mlp_act, 1)
            for h in range(2):
                act.wait_ge(mlp_mm, 12 + h + 1)
                nc.scalar.activation(y_sb[:, h * BANK:(h + 1) * BANK], rep[0:1, h, 0:BANK], ACT.Copy)\
                  .then_inc(mlp_act, 1)

        @block.vector
        def _(dve):
            def split(j, T=0):
                dve.wait_ge(rows_in, 16 * FIELDS * (j + 1) + 16 * FIELDS * T)
                if j >= 1:
                    dve.wait_ge(parts_turned, 2 * j + 2 * T)
                x = gathered[:, :, :].rearrange("p f d -> p d f")
                nc.vector.tensor_copy(parts_b[:, :, 0, :], x).then_inc(split_step, 1)
                dve.wait_ge(split_step, 3 * j + 1 + 3 * T)
                nc.vector.tensor_tensor(rest_b[:, :, :], x, parts_b[:, :, 0, :], ALU.subtract).then_inc(split_step, 1)
                dve.wait_ge(split_step, 3 * j + 2 + 3 * T)
                nc.vector.tensor_copy(parts_b[:, :, 1, :], rest_b[:, :, :]).then_inc(split_step, 1)
                dve.wait_ge(split_step, 3 * j + 3 + 3 * T)
                nc.vector.tensor_tensor(parts_b[:, :, 2, :], rest_b[:, :, :], parts_b[:, :, 1, :],
                                        ALU.subtract).then_inc(parts_ready, 1)

            def product(n, T=0):
                k, layer, c, q = place(n)
                rows, buf = (P if layer else rows0(c)), n % NBUF
                dve.wait_ge(rep_done, n + 1 + BODY * T)
                if c == 0:
                    dve.wait_ge(*((hid_done, k + 2 * T) if layer else (copies_kept, k + 1 + 2 * T)))
                if n >= NBUF:
                    who = LOW[place(n - NBUF)[3]]
                    if who == "-":
                        dve.wait_ge(main_done, n - NBUF + 1 + BODY * T)
                    if who == "p":
                        dve.wait_ge(low_p_done, through("p", n - NBUF, T))
                other = hidden[:, (k - 1) % 2, :] if layer else x_copies[0:rows, k % 2, :]
                nc.vector.tensor_tensor(z[0:rows, buf, :], rep[0:rows, n % 2, :], other, ALU.mult)\
                  .then_inc(prod_done, 1)

            def low(n, T=0):
                k, layer, c, q = place(n)
                if LOW[q] != "v":
                    return
                dve.wait_ge(high_done, through("high", n, T))
                if n >= NBUF:
                    dve.wait_ge(main_done, n - NBUF + 1 + BODY * T)
                rows, buf = (P if layer else rows0(c)), n % NBUF
                nc.vector.tensor_tensor(z_low[0:rows, buf, :], z[0:rows, buf, :],
                                        z_high[0:rows, buf, :].bitcast(F32), ALU.subtract).then_inc(low_v_done, 1)

            def sum_d(dst, src):
                return nc.vector.tensor_reduce(dst, src.rearrange("p h (d b) -> p b (h d)", b=P), AX.X, ALU.add)

            def sum_direct(j, T=0):
                dve.wait_ge(hid_done, 2 * j + 2 + 2 * T)
                sum_d(top_dir[0:HID, bass.ds(j * P + P * T, P)], direct0[:, :, :]).then_inc(direct_summed, 1)

            def sum_cur(j, T=0):
                dve.wait_ge(cur1_done, 2 * j + 2 + 2 * T)
                sum_d(top_cur[:, bass.ds(j * P + P * T, P)], cur1[:, :, :]).then_inc(cur_summed, 1)

            def step(n, T=0):
                k, layer, c, q = place(n)
                if n + PROD_AHEAD < CHUNKS:
                    product(n + PROD_AHEAD, T)
                if n + LOW_AHEAD < CHUNKS:
                    low(n + LOW_AHEAD, T)
                if k % 2 and q == Q_SPLIT and (k + 1) // 2 < GROUPS:
                    split((k + 1) // 2, T)
                if k % 2 and k >= 3 and q == Q_SUM:
                    sum_cur((k - 3) // 2, T)
                if k % 2 and q == Q_COPIES:
                    sum_direct((k - 1) // 2, T)

            dve.wait_ge(weights_in, 48)
            nc.vector.tensor_tensor(w0_sb[:, :, :], w0_sb[:, :, :], w0_t[:, :, :], ALU.add).then_inc(w_summed, 1)
            dve.wait_ge(w_high_done, 2)
            nc.vector.tensor_tensor(w0_low[:, :, :], w0_sb[:, :, :], w0_high[:, :, :].bitcast(F32),
                                    ALU.subtract).then_inc(w_low_done, 1)
            nc.vector.tensor_tensor(w1_low[:, :, :], w1_sb[:, :, :], w1_high[:, :, :].bitcast(F32),
                                    ALU.subtract).then_inc(w_low_done, 1)
            split(0)
            for n in range(PROD_AHEAD):
                product(n)
                if n >= PROD_AHEAD - LOW_AHEAD:
                    low(n - PROD_AHEAD + LOW_AHEAD)
            for n in range(FIRST):
                step(n)
            with dve.Fori(0, BODIES - 1) as T:
                for n in range(FIRST, FIRST + BODY):
                    step(n, T)
            for n in range(LAST, CHUNKS):
                step(n)
            sum_cur(GROUPS - 1)

            dve.wait_ge(top_in, 128)
            for h in range(2):
                cols = slice(h * BANK, (h + 1) * BANK)
                for m in (1, 3):
                    dve.wait_ge(mlp_mm, 4 * h + m + 1)
                    src = (acc0, acc1)[m // 2][:, BANK:] if h == 0 else rep[:, m // 2, BANK:]
                    nc.vector.tensor_scalar(mlp1[:, m, cols], src, bt1_sb[:, m:m + 1], 0.0, ALU.add, ALU.max)\
                      .then_inc(mlp_vec, 1)
            for h in range(2):
                cols = slice(h * BANK, (h + 1) * BANK)
                dve.wait_ge(mlp_mm, 8 + 2 * h + 2)
                nc.vector.tensor_scalar(mlp2[:, 1, cols], (acc0, acc1)[h][:, BANK:], bt2_sb[:, 1:2], 0.0,
                                        ALU.add, ALU.max).then_inc(mlp_vec, 1)

        @block.tensor
        def _(pe):
            def turn(k_tile, of, T=0):
                group = k_tile // 2
                src, eye, ready, done = {
                    "copies": (copies_b, eye32_sb, copies_ready, copies_turned),
                    "parts": (parts_b, eye16_sb, parts_ready, parts_turned)}[of]
                pe.wait_ge(ready, group + 1 + T)
                if k_tile >= 2:
                    pe.wait_ge(*((hid_done, k_tile + 2 * T) if of == "copies" else (copies_kept, k_tile + 1 + 2 * T)))
                to = turned_to(k_tile, of)
                for d in range(DT):
                    last = nc.tensor.transpose(to[0:K0, d * P:(d + 1) * P],
                                               src[:, (k_tile % 2) * DT + d, :, :], eye[:, :])
                last.then_inc(done, 1)

            def repeat(n, T=0):
                k, layer, c, q = place(n)
                if layer == 0 and c == 0:
                    pe.wait_ge(parts_kept, k + 1 + 2 * T)
                if n == 1:
                    pe.wait_ge(parts_kept, 2)
                if n >= 2:
                    pe.wait_ge(prod_done, n - 1 + BODY * T)
                sel, half = (sel1_sb, (k - 1) % 2) if layer else (sel0_sb, k % 2)
                for h in range(0, TILE, BANK):
                    last = nc.tensor.matmul(rep[:, n % 2, h:h + BANK], sel[:, c, :],
                                            x_parts[:, half, h:h + BANK], start=True, stop=True)
                last.then_inc(rep_done, 1)

            def weigh(n, T=0):
                k, layer, c, q = place(n)
                rows, buf = (P if layer else rows0(c)), n % NBUF
                if LOW[q] == "-":
                    pe.wait_ge(prod_done, n + 1 + BODY * T)
                elif LOW[q] == "v":
                    pe.wait_ge(low_v_done, through("v", n, T))
                else:
                    pe.wait_ge(low_p_done, through("p", n, T))
                if c == 0 and layer == 0:
                    pe.wait_ge(parts_kept, max(k + 1, 2) + 2 * T)
                    pe.wait_ge(copies_kept, max(k + 1, 2) + 2 * T)
                    if k >= 1:
                        pe.wait_ge(hid_done, k + 2 * T)
                if c == 0 and layer == 1 and k >= 2:
                    pe.wait_ge(cur1_done, k - 1 + 2 * T)
                acc = acc1 if layer else acc0
                last_c = C1 - 1 if layer else C0 - 1
                if LOW[q] == "-":
                    passes = [(w1_sb if layer else w0_sb, z)]
                else:
                    high, low = (w1_high, w1_low) if layer else (w0_high, w0_low)
                    passes = [(high, z_high), (low, z_high), (high, z_low)]
                for i, (w, zz) in enumerate(passes):
                    for h in range(0, TILE, BANK):
                        last = nc.tensor.matmul(acc[:, h:h + BANK], w[0:rows, c, :], zz[0:rows, buf, h:h + BANK],
                                                start=(c == 0 and i == 0),
                                                stop=(c == last_c and i == len(passes) - 1))
                last.then_inc(main_done, 1)

            def step(n, T=0):
                k, layer, c, q = place(n)
                weigh(n, T)
                if n + REP_AHEAD < CHUNKS:
                    repeat(n + REP_AHEAD, T)
                if 1 <= k < TILES - 1:
                    if q == Q_COPIES - 1:
                        turn(k + 1, "copies", T)
                    if q == Q_TURN:
                        turn(k + 1, "parts", T)

            pe.wait_ge(eye_in, 32)
            pe.wait_ge(sel_in, 32)
            for k_tile in range(2):
                turn(k_tile, "copies")
                turn(k_tile, "parts")
            for n in range(REP_AHEAD):
                if n == 2:
                    break
                repeat(n)
            pe.wait_ge(w_low_done, 2)
            for n in range(2, REP_AHEAD):
                repeat(n)
            for n in range(FIRST):
                step(n)
            with pe.Fori(0, BODIES - 1) as T:
                for n in range(FIRST, FIRST + BODY):
                    step(n, T)
            for n in range(LAST, CHUNKS):
                step(n)

            pe.wait_ge(top_in, 128)
            pe.wait_ge(direct_summed, GROUPS)
            pe.wait_ge(cur_summed, GROUPS)
            for h in range(2):
                cols = slice(h * BANK, (h + 1) * BANK)
                for m in range(H1 // P):
                    space = (acc0, acc1)[m // 2] if h == 0 else rep[:, m // 2, :]
                    out = space[:, (m % 2) * BANK:(m % 2 + 1) * BANK]
                    nc.tensor.matmul(out, wt1_cur[:, m * P:(m + 1) * P], top_cur[:, cols], start=True, stop=False)
                    nc.tensor.matmul(out, wt1_dir[:, m * P:(m + 1) * P], top_dir[:, cols], start=False, stop=True)\
                      .then_inc(mlp_mm, 1)
            for h in range(2):
                cols = slice(h * BANK, (h + 1) * BANK)
                pe.wait_ge(mlp_act, 2 * h + 2)
                pe.wait_ge(mlp_vec, 2 * h + 2)
                for m in range(H2 // P):
                    out = (acc0, acc1)[h][:, m * BANK:(m + 1) * BANK]
                    for c in range(H1 // P):
                        last = nc.tensor.matmul(out, wt2_sb[:, c, m * P:(m + 1) * P], mlp1[:, c, cols],
                                                start=(c == 0), stop=(c == H1 // P - 1))
                    last.then_inc(mlp_mm, 1)
            for h in range(2):
                cols = slice(h * BANK, (h + 1) * BANK)
                pe.wait_ge(mlp_act, 4 + h + 1)
                pe.wait_ge(mlp_vec, 4 + h + 1)
                for c in range(H2 // P):
                    last = nc.tensor.matmul(rep[0:1, h, 0:BANK], wt3_sb[:, c:c + 1], mlp2[:, c, cols],
                                            start=(c == 0), stop=(c == H2 // P - 1))
                last.then_inc(mlp_mm, 1)


def layout():
    shifts = list(range(1, SHIFTS - 1)) + [0, SHIFTS - 1]
    pair_a, pair_b = np.full((K0, C0), FIELDS * FIELDS), np.full((K0, C0), FIELDS * FIELDS)
    sel0, sel1 = np.zeros((3, FIELDS, C0, P)), np.zeros((3, FIELDS, C1, P))
    for at, s in enumerate(shifts):
        c, r = divmod(at, PER0)
        for j in range(FIELDS):
            i = (j + s) % FIELDS
            pair_a[r * FIELDS + j, c] = i * FIELDS + j
            if s:
                pair_b[r * FIELDS + j, c] = j * FIELDS + i
            sel0[:, i, c, r * FIELDS + j] = 1
    for i in range(FIELDS):
        sel1[:, i, i // 2, (i % 2) * HID:(i % 2 + 1) * HID] = 1
    return pair_a, pair_b, sel0.reshape(K0, C0, P), sel1.reshape(K0, C1, P)


def kernel(**inputs):
    import concourse.bacc as bacc
    import ml_dtypes
    from concourse.bass_utils import run_bass_kernel_spmd

    a = {k: np.asarray(v) for k, v in inputs.items()}
    pair_a, pair_b, sel0, sel1 = layout()
    w0 = np.concatenate([a["L0_rec_W0"], np.zeros((1, L), np.float32)])
    w1 = np.concatenate([a["L0_rec_W1"], np.zeros((C1 * P - FIELDS * HID, L), np.float32)])
    arrays = {
        "dense_t": a["dense_ctx"].T,
        "ids": a["ids"].reshape(GROUPS, P, FIELDS),
        **{f"tbl_{f}": a[f"tbl_{f}"] for f in range(FIELDS)},
        "w0_a": w0[pair_a], "w0_b": w0[pair_b],
        "w1": w1.reshape(C1, P, L).transpose(1, 0, 2),
        "sel0": sel0.astype(ml_dtypes.bfloat16), "sel1": sel1.astype(ml_dtypes.bfloat16),
        "eye16": np.eye(P, dtype=ml_dtypes.bfloat16), "eye32": np.eye(P, dtype=np.float32),
        "wt1": a["W_top1"], "bt1": a["b_top1"].reshape(H1 // P, P).T,
        "wt2": a["W_top2"].reshape(H1 // P, P, H2).transpose(1, 0, 2), "bt2": a["b_top2"].reshape(H2 // P, P).T,
        "wt3": a["W_top3"].reshape(H2 // P, P).T,
    }
    arrays = {k: np.ascontiguousarray(v) for k, v in arrays.items()}
    nc = bacc.Bacc("TRN2", target_bir_lowering=False, num_devices=1)
    ap = {k: nc.dram_tensor(k, v.shape, mybir.dt.from_np(v.dtype), kind="ExternalInput").ap()
          for k, v in arrays.items()}
    y = nc.dram_tensor("y", (1, B), F32, kind="ExternalOutput").ap()
    tables = [ap.pop(f"tbl_{f}") for f in range(FIELDS)]
    program(nc, tables=tables, y=y, **ap)
    r = run_bass_kernel_spmd(nc, [arrays], core_ids=[0])
    return r.results[0]["y"].reshape(B, 1)
```

```python
from contextlib import ExitStack

import numpy as np

import concourse.bass as bass
from concourse import mybir

F32 = mybir.dt.float32
F32R = mybir.dt.float32r
BF16 = mybir.dt.bfloat16
I32 = mybir.dt.int32
ALU = mybir.AluOpType
ACT = mybir.ActivationFunctionType
AX = mybir.AxisListType

P = 128
B, FIELDS, D = 1024, 39, 16
L = 128
HID = L // 2
DENSE, H1, H2 = 16, 512, 256
GROUPS = B // P
DT = D // 2
TILE = DT * P
BANK = 512
TILES = 2 * GROUPS
SHIFTS = FIELDS // 2 + 1
PER0 = P // FIELDS
C0 = -(-SHIFTS // PER0)
C1 = -(-FIELDS // 2)
K0 = PER0 * FIELDS
BLOCK = C0 + C1
CHUNKS = TILES * BLOCK
BODY = 2 * BLOCK
FIRST = C0 + BLOCK
BODIES = GROUPS - 1
LAST = FIRST + (BODIES - 1) * BODY
TAIL = FIRST + BODIES * BODY
NZ, NBUF = 6, 9

LOW = "vvp-p-vvvp-vpvvpvpvvpvv-pvv" \
      "pv-pvp-p-vv-p-v-pvvpv-p-vvv"
LOW_EARLY = "---vv--" "-vv-v-v--vvpvpvpp-pvvvppvp-"
LOW_LAST = "pvvvvvvvvvvvvvvvvvvv"
OVER = 15
REP_AHEAD, PROD_AHEAD, HIGH_AHEAD, LOW_AHEAD = 6, 5, 4, 3
Q_ROWS, Q_SPLIT, Q_REST, Q_TURN, Q_NEXT = 10, 11, 13, 15, 17
Q_HID, Q_SUM, Q_KEEP = C0 - 1, 3, 20
Q_DIRECT = 0
TURN_EACH, PIECES = 4, 2
Q_GATHER = next(q for q in range(Q_REST + 1, BLOCK) if LOW[BLOCK + q + LOW_AHEAD] == "p")


def rows_of(layer, c):
    if layer:
        return HID * (min(FIELDS, 2 * c + 2) - 2 * c)
    return FIELDS * (min(SHIFTS, PER0 * c + PER0) - PER0 * c)


def folded(layer, c):
    return layer == 1 and 2 * rows_of(layer, c) <= P


MULTIPLY_AT = {0: [0], 1: [1], 3: [2], 4: [3], 6: [4], 7: [4], 8: [5], 9: [5], 12: [6]}
RESULT_AT = {1: 0, 2: 1, 4: 2, 5: 3, 8: 4, 10: 5, 13: 6}


def place(n):
    k, q = (0, n) if n < C0 else (1 + (n - C0) // BLOCK, (n - C0) % BLOCK)
    if n >= TAIL:
        k, q = 2 * BODIES + 2, n - TAIL + C0
    return (k, 0, q, q) if q < C0 else (k, 1, q - C0, q)


def kind(n):
    if n >= TAIL:
        return LOW_LAST[n - TAIL]
    return LOW_EARLY[n] if n < FIRST else LOW[(place(n)[0] % 2) * BLOCK + place(n)[3]]


def counts(wanted):
    out = [0]
    for n in range(CHUNKS):
        out.append(out[-1] + wanted(kind(n)))
    return out


BEFORE = {who: counts(lambda w, who=who: w == who) for who in "vp"}
BEFORE["high"] = counts(lambda w: w != "-")


def through(what, n, T):
    before = BEFORE[what]
    return before[n + 1] + (before[FIRST + BODY] - before[FIRST]) * T


def program(nc, dense_t, ids, tables, w0_a, w0_b, w1, sel0, sel1, eye16,
            wt1, bt1, wt2, bt2, wt3, y):
    with ExitStack() as ctx:
        def sb(name, shape, dt):
            return ctx.enter_context(nc.sbuf_tensor(name, shape, dt))

        def psum(name, shape, dt):
            return ctx.enter_context(nc.psum_tensor(name, shape, dt))

        def sem(name):
            return ctx.enter_context(nc.semaphore(name))

        w0_sb = sb("w0_sb", [K0, C0, L], F32)
        w0_high, w0_low = sb("w0_high", [K0, C0, L], F32R), sb("w0_low", [K0, C0, L], F32R)
        w1_sb = sb("w1_sb", [P, C1, L], F32)
        w1_high, w1_low = sb("w1_high", [P, C1, L], F32R), sb("w1_low", [P, C1, L], F32R)
        sel0_sb, sel1_sb = sb("sel0_sb", [K0, C0 + 1, P], BF16), sb("sel1_sb", [K0, C1, P], BF16)
        eye16_sb = sb("eye16_sb", [P, P], BF16)
        wt3_sb = sb("wt3_sb", [P, H2 // P], F32)
        bt1_sb, bt2_sb = sb("bt1_sb", [P, H1 // P], F32), sb("bt2_sb", [P, H2 // P], F32)

        ids_sb = sb("ids_sb", [P, FIELDS], I32)
        gathered = sb("gathered", [P, FIELDS, D], F32)
        parts_b = sb("parts_b", [P, D, 3, FIELDS], BF16)
        rest_b = gathered[:, :, :].rearrange("p f d -> p d f")

        x_copies = sb("x_copies", [P, 2, TILE], F32)
        x_parts = sb("x_parts", [K0, 2, TILE], BF16)
        x_next = sb("x_next", [K0, TILE], BF16)
        hidden = sb("hidden", [P, 2, TILE], F32)

        z = sb("z", [P, NZ, TILE], F32)
        z_high, z_low = sb("z_high", [P, NBUF, TILE], F32R), sb("z_low", [P, NBUF, TILE], F32R)

        direct0, cur1 = sb("direct0", [HID, 2, TILE], F32), sb("cur1", [P, 2, TILE], F32)
        top_dir, top_cur = sb("top_dir", [HID + DENSE, B], F32), sb("top_cur", [P, B], F32)
        w0_t = z[0:K0, 0, 0:C0 * L].rearrange("p (c l) -> p c l", c=C0)
        wt1_cur, wt1_dir = x_copies[:, 0, 0:H1], x_copies[0:HID + DENSE, 0, H1:2 * H1]
        wt2_sb = x_copies[:, 1, :].rearrange("p (c n) -> p c n", c=H1 // P)
        first_rows = sb("first_rows", [P, 3, BANK], F32)
        mlp1 = ([first_rows[:, m, :] for m in range(3)] + [hidden[:, 0, 0:BANK]],
                [z[:, m, 0:BANK] for m in range(H1 // P)])
        mlp2 = ([hidden[:, 0, BANK:], gathered[:, :, :].rearrange("p f d -> p (f d)")[:, 0:BANK]],
                [z[:, H1 // P + m, 0:BANK] for m in range(H2 // P)])
        y_sb = sb("y_sb", [1, B], F32)

        acc0, acc1 = psum("acc0", [P, TILE], F32), psum("acc1", [P, TILE], F32)
        rep = psum("rep", [P, 2, TILE], F32)

        weights_in, sel_in, eye_in, top_in = sem("weights_in"), sem("sel_in"), sem("eye_in"), sem("top_in")
        w_summed, w_high_done, w_low_done = sem("w_summed"), sem("w_high_done"), sem("w_low_done")
        ids_in, rows_in = sem("ids_in"), sem("rows_in")
        split_step = sem("split_step")
        first_part = sem("first_part")
        parts_ready = sem("parts_ready")
        parts_turned, copies_turned = sem("parts_turned"), sem("copies_turned")
        parts_kept, copies_kept = sem("parts_kept"), sem("copies_kept")
        next_kept = sem("next_kept")
        rep_done, prod_done, main_done = sem("rep_done"), sem("prod_done"), sem("main_done")
        high_done, low_v_done, low_p_done = sem("high_done"), sem("low_v_done"), sem("low_p_done")
        hid_done, cur1_done = sem("hid_done"), sem("cur1_done")
        direct_summed, cur_summed = sem("direct_summed"), sem("cur_summed")
        mlp_mm, mlp_act, mlp_vec, y_out = sem("mlp_mm"), sem("mlp_act"), sem("mlp_vec"), sem("y_out")

        block = ctx.enter_context(nc.Block())

        def low_at(n):
            k, layer, c, q = place(n)
            rows, buf = rows_of(layer, c), n % NBUF
            return z_high[rows:2 * rows, buf, :] if folded(layer, c) else z_low[0:rows, buf, :]

        def acc_of(k, layer):
            return acc1 if layer or k == 0 else acc0

        def turned_to(k_tile):
            return (rep[:, k_tile, 0:BANK] if k_tile < 2 else acc0[:, 0:BANK]).bitcast(BF16)

        def copied_to(k_tile):
            return acc1 if k_tile == 0 else acc0

        @block.sync
        def _(sp):
            sp.dma_start(ids_sb[:, :], ids[0, :, :]).then_inc(ids_in, 16)
            for dst, src in ((w0_sb[:, :, :], w0_a), (w0_t, w0_b), (w1_sb[:, :, :], w1)):
                sp.dma_start(dst, src).then_inc(weights_in, 16)
            sp.dma_start(eye16_sb[:, :], eye16).then_inc(eye_in, 16)
            for dst, src in ((sel0_sb, sel0), (sel1_sb, sel1)):
                sp.dma_start(dst[:, :, :], src).then_inc(sel_in, 16)
            for dst, src in ((top_dir[HID:, :], dense_t), (wt3_sb[:, :], wt3),
                             (bt1_sb[:, :], bt1), (bt2_sb[:, :], bt2)):
                sp.dma_start(dst, src).then_inc(top_in, 16)
            with sp.Fori(1, GROUPS) as j:
                sp.wait_ge(rows_in, j * (16 * FIELDS))
                sp.dma_start(ids_sb[:, :], ids[bass.ds(j, 1), :, :].rearrange("j p f -> (j p) f"))\
                  .then_inc(ids_in, 16)
            sp.wait_ge(prod_done, TAIL - C1)
            for dst, src in ((wt1_cur, wt1[HID:HID + L, :]), (wt1_dir[0:HID, :], wt1[0:HID, :]),
                             (wt1_dir[HID:, :], wt1[HID + L:, :]), (wt2_sb, wt2)):
                sp.dma_start(dst, src).then_inc(top_in, 16)
            for h in range(2):
                sp.wait_ge(mlp_act, (7, 11)[h])
                sp.dma_start(y[:, h * BANK:(h + 1) * BANK], y_sb[:, h * BANK:(h + 1) * BANK])\
                  .then_inc(y_out, 16)
            sp.wait_ge(y_out, 32)

        @block.gpsimd
        def _(pool):
            def gather(f):
                pool.indirect_dma_start(
                    out=gathered[:, f, :], out_offset=None, in_=tables[f],
                    in_offset=bass.IndirectOffsetOnAxis(ap=ids_sb[:, f:f + 1], axis=0)).then_inc(rows_in, 16)

            def low(n, T):
                pool.wait_ge(high_done, through("high", n, T))
                if n >= NBUF:
                    pool.wait_ge(main_done, n - NBUF + 1 + BODY * T)
                k, layer, c, q = place(n)
                rows, buf = rows_of(layer, c), n % NBUF
                pool.tensor_tensor(low_at(n), z[0:rows, n % NZ, :],
                                   z_high[0:rows, buf, :].bitcast(F32), ALU.subtract).then_inc(low_p_done, 1)

            def step(n, T=0):
                k, layer, c, q = place(n)
                group = (k + 3) // 2 if k % 2 and q >= Q_GATHER else (k + 2) // 2
                if k % 2 and q == Q_GATHER and group < GROUPS:
                    pool.wait_ge(parts_ready, group + T)
                    pool.wait_ge(ids_in, 16 * (group + 1) + 16 * T)
                if n + LOW_AHEAD < CHUNKS and kind(n + LOW_AHEAD) == "p":
                    low(n + LOW_AHEAD, T)
                if group in range(2, GROUPS):
                    at = (q - Q_GATHER) % BLOCK if k % 2 and q >= Q_GATHER else \
                        q + (BLOCK - Q_GATHER if k % 2 == 0 else BODY - Q_GATHER)
                    room = BODY - Q_GATHER + Q_ROWS
                    for f in range(at * FIELDS // room, min(at + 1, room) * FIELDS // room):
                        gather(f)

            pool.wait_ge(ids_in, 16)
            for f in range(FIELDS):
                gather(f)
            pool.wait_ge(parts_ready, 1)
            pool.wait_ge(ids_in, 32)
            for n in range(LOW_AHEAD):
                if kind(n) == "p":
                    low(n, 0)
            for n in range(FIRST):
                step(n)
                if n < OVER:
                    for f in range(n * FIELDS // OVER, (n + 1) * FIELDS // OVER):
                        gather(f)
            with pool.Fori(0, BODIES - 2) as T:
                for n in range(FIRST, FIRST + BODY):
                    step(n, T)
            for n in range(LAST - BODY, CHUNKS):
                step(n)

        @block.scalar
        def _(act):
            def first_parts(j, T=0):
                act.wait_ge(rows_in, 16 * FIELDS * (j + 1) + 16 * FIELDS * T)
                if j >= 1:
                    act.wait_ge(parts_turned, 2 * j + 2 * T)
                nc.scalar.activation(parts_b[:, :, 0, :], gathered[:, :, :].rearrange("p f d -> p d f"),
                                     ACT.Copy).then_inc(first_part, 1)

            def keep_next(k_tile, T=0):
                act.wait_ge(parts_turned, k_tile + 1 + 2 * T)
                nc.scalar.activation(x_next[:, :], turned_to(k_tile)[0:K0, :], ACT.Copy).then_inc(next_kept, 1)

            def keep_parts(k_tile, T=0):
                if k_tile < 2:
                    act.wait_ge(parts_turned, k_tile + 1)
                    src = turned_to(k_tile)[0:K0, :]
                else:
                    act.wait_ge(next_kept, k_tile - 1 + 2 * T)
                    src = x_next[:, :]
                nc.scalar.activation(x_parts[:, k_tile % 2, :], src, ACT.Copy).then_inc(parts_kept, 1)

            def keep_copies(k_tile, T=0):
                act.wait_ge(copies_turned, k_tile + 1 + 2 * T)
                nc.scalar.activation(x_copies[0:K0, k_tile % 2, :], copied_to(k_tile)[0:K0, :],
                                     ACT.Copy).then_inc(copies_kept, 1)

            def high(n, T=0):
                k, layer, c, q = place(n)
                if kind(n) == "-":
                    return
                act.wait_ge(prod_done, n + 1 + BODY * T)
                if n >= NBUF:
                    act.wait_ge(main_done, n - NBUF + 1 + BODY * T)
                rows, buf = rows_of(layer, c), n % NBUF
                nc.scalar.activation(z_high[0:rows, buf, :], z[0:rows, n % NZ, :], ACT.Copy).then_inc(high_done, 1)

            def keep_layer0(k, n, T):
                act.wait_ge(main_done, n + 1 + BODY * T)
                if k >= 2:
                    act.wait_ge(prod_done, n - Q_HID + BODY * T)
                if k >= 2 and k % 2 == 0:
                    act.wait_ge(direct_summed, k // 2 + T)
                half, acc = k % 2, acc_of(k, 0)
                nc.scalar.activation(hidden[0:HID, half, :], acc[0:HID, :], ACT.Relu)
                nc.scalar.activation(hidden[HID:P, half, :], acc[0:HID, :], ACT.Relu)
                nc.scalar.activation(direct0[:, half, :], acc[HID:P, :], ACT.Relu).then_inc(hid_done, 1)

            def keep_layer1(k, n, T):
                act.wait_ge(main_done, n + 1 + BODY * T)
                if k >= 3 and (k - 1) % 2 == 0:
                    act.wait_ge(cur_summed, (k - 1) // 2 + T)
                nc.scalar.activation(cur1[:, (k - 1) % 2, :], acc1[:, :], ACT.Relu).then_inc(cur1_done, 1)

            def keep_result(at):
                if at == 0:
                    act.wait_ge(top_in, 128)
                act.wait_ge(mlp_mm, at + 1)
                if at < 4:
                    nc.scalar.activation(mlp1[0][at], acc0[:, (at % 2) * BANK:(at % 2 + 1) * BANK], ACT.Relu,
                                         bias=bt1_sb[:, at:at + 1]).then_inc(mlp_act, 1)
                elif at < 6:
                    nc.scalar.activation(mlp2[0][at - 4], acc0[:, (at % 2) * BANK:(at % 2 + 1) * BANK], ACT.Relu,
                                         bias=bt2_sb[:, at - 4:at - 3]).then_inc(mlp_act, 1)
                else:
                    nc.scalar.activation(y_sb[:, 0:BANK], acc0[0:1, 0:BANK], ACT.Copy).then_inc(mlp_act, 1)

            def step(n, T=0):
                k, layer, c, q = place(n)
                if n + HIGH_AHEAD < CHUNKS:
                    high(n + HIGH_AHEAD, T)
                if layer == 0 and q == Q_HID:
                    keep_layer0(k, n, T)
                if k % 2 and q == Q_SPLIT and (k + 1) // 2 < GROUPS:
                    first_parts((k + 1) // 2, T)
                if 1 <= k < TILES - 1:
                    if q == Q_NEXT:
                        keep_next(k + 1, T)
                    if q == Q_NEXT + 2:
                        keep_copies(k + 1, T)
                    if q == Q_KEEP:
                        act.wait_ge(rep_done, n - q + BLOCK + BODY * T)
                        keep_parts(k + 1, T)
                if q == BLOCK - 1:
                    keep_layer1(k, n, T)
                if n - TAIL in RESULT_AT:
                    keep_result(RESULT_AT[n - TAIL])

            act.wait_ge(w_summed, 1)
            nc.scalar.activation(w0_high[:, :, :], w0_sb[:, :, :], ACT.Copy).then_inc(w_high_done, 1)
            act.wait_ge(weights_in, 48)
            nc.scalar.activation(w1_high[:, :, :], w1_sb[:, :, :], ACT.Copy).then_inc(w_high_done, 1)
            first_parts(0)
            for k_tile in range(2):
                keep_parts(k_tile)
                keep_copies(k_tile)
            for n in range(HIGH_AHEAD):
                high(n)
            for n in range(FIRST):
                step(n)
            with act.Fori(0, BODIES - 1) as T:
                for n in range(FIRST, FIRST + BODY):
                    step(n, T)
            for n in range(LAST, CHUNKS):
                step(n)

            for m in (0, 2):
                act.wait_ge(mlp_mm, 7 + m + 1)
                nc.scalar.activation(mlp1[1][m], (acc0, rep[:, 0, :])[m // 2][:, 0:BANK], ACT.Relu,
                                     bias=bt1_sb[:, m:m + 1]).then_inc(mlp_act, 1)
            act.wait_ge(mlp_mm, 12)
            nc.scalar.activation(mlp2[1][0], rep[:, 1, 0:BANK], ACT.Relu, bias=bt2_sb[:, 0:1]).then_inc(mlp_act, 1)
            act.wait_ge(mlp_mm, 14)
            nc.scalar.activation(y_sb[:, BANK:], acc0[0:1, 0:BANK], ACT.Copy).then_inc(mlp_act, 1)

        @block.vector
        def _(dve):
            def split(j, T=0):
                dve.wait_ge(rows_in, 16 * FIELDS * (j + 1) + 16 * FIELDS * T)
                if j >= 1:
                    dve.wait_ge(parts_turned, 2 * j + 2 * T)
                dve.wait_ge(first_part, j + 1 + T)
                nc.vector.tensor_tensor(rest_b, rest_b, parts_b[:, :, 0, :], ALU.subtract).then_inc(split_step, 1)
                dve.wait_ge(split_step, 2 * j + 1 + 2 * T)
                nc.vector.tensor_copy(parts_b[:, :, 1, :], rest_b).then_inc(split_step, 1)
                dve.wait_ge(split_step, 2 * j + 2 + 2 * T)
                nc.vector.tensor_tensor(parts_b[:, :, 2, :], rest_b, parts_b[:, :, 1, :],
                                        ALU.subtract).then_inc(parts_ready, 1)

            def product(n, T=0):
                k, layer, c, q = place(n)
                rows, buf = rows_of(layer, c), n % NBUF
                dve.wait_ge(rep_done, n + 1 + BODY * T)
                if c == 0:
                    dve.wait_ge(*((hid_done, k + 2 * T) if layer else (copies_kept, k + 1 + 2 * T)))
                if n >= NZ:
                    who = kind(n - NZ)
                    if who == "-":
                        dve.wait_ge(main_done, n - NZ + 1 + BODY * T)
                    if who == "p":
                        dve.wait_ge(low_p_done, through("p", n - NZ, T))
                other = hidden[0:rows, (k - 1) % 2, :] if layer else x_copies[0:rows, k % 2, :]
                nc.vector.tensor_tensor(z[0:rows, n % NZ, :], rep[0:rows, n % 2, :], other, ALU.mult)\
                  .then_inc(prod_done, 1)

            def low(n, T=0):
                k, layer, c, q = place(n)
                if kind(n) != "v":
                    return
                dve.wait_ge(high_done, through("high", n, T))
                if n >= NBUF:
                    dve.wait_ge(main_done, n - NBUF + 1 + BODY * T)
                rows, buf = rows_of(layer, c), n % NBUF
                nc.vector.tensor_tensor(low_at(n), z[0:rows, n % NZ, :],
                                        z_high[0:rows, buf, :].bitcast(F32), ALU.subtract).then_inc(low_v_done, 1)

            def sum_d(dst, src, j, i, T):
                size = P // PIECES
                return nc.vector.tensor_reduce(
                    dst[:, bass.ds(j * P + i * size + P * T, size)],
                    src.rearrange("p h (d b) -> p b (h d)", b=P)[:, i * size:(i + 1) * size, :], AX.X, ALU.add)

            def sum_direct(j, i, T=0):
                dve.wait_ge(hid_done, 2 * j + 2 + 2 * T)
                last = sum_d(top_dir[0:HID, :], direct0[:, :, :], j, i, T)
                if i == PIECES - 1:
                    last.then_inc(direct_summed, 1)

            def sum_cur(j, i, T=0):
                dve.wait_ge(cur1_done, 2 * j + 2 + 2 * T)
                last = sum_d(top_cur[:, :], cur1[:, :, :], j, i, T)
                if i == PIECES - 1:
                    last.then_inc(cur_summed, 1)

            def step(n, T=0):
                k, layer, c, q = place(n)
                if n + PROD_AHEAD < CHUNKS:
                    product(n + PROD_AHEAD, T)
                if n + LOW_AHEAD < CHUNKS:
                    low(n + LOW_AHEAD, T)
                if k % 2 and q == Q_REST and (k + 1) // 2 < GROUPS:
                    split((k + 1) // 2, T)
                if k % 2 and k >= 3 and 0 <= q - Q_SUM < PIECES:
                    sum_cur((k - 3) // 2, q - Q_SUM, T)
                first = C0 if k == TILES else Q_DIRECT
                if k % 2 == 0 and k >= 2 and 0 <= q - first < PIECES:
                    sum_direct((k - 2) // 2, q - first, T)

            dve.wait_ge(weights_in, 48)
            nc.vector.tensor_tensor(w0_sb[:, :, :], w0_sb[:, :, :], w0_t, ALU.add).then_inc(w_summed, 1)
            dve.wait_ge(w_high_done, 2)
            nc.vector.tensor_tensor(w0_low[:, :, :], w0_sb[:, :, :], w0_high[:, :, :].bitcast(F32),
                                    ALU.subtract).then_inc(w_low_done, 1)
            nc.vector.tensor_tensor(w1_low[:, 0:C1 - 1, :], w1_sb[:, 0:C1 - 1, :],
                                    w1_high[:, 0:C1 - 1, :].bitcast(F32), ALU.subtract).then_inc(w_low_done, 1)
            nc.vector.tensor_tensor(w1_low[0:HID, C1 - 1, :], w1_sb[0:HID, C1 - 1, :],
                                    w1_high[0:HID, C1 - 1, :].bitcast(F32), ALU.subtract).then_inc(w_low_done, 1)
            nc.vector.tensor_copy(w1_low[HID:P, C1 - 1, :], w1_high[HID:P, C1 - 1, :].bitcast(F32))\
              .then_inc(w_low_done, 1)
            split(0)
            for n in range(PROD_AHEAD):
                product(n)
                if n >= PROD_AHEAD - LOW_AHEAD:
                    low(n - PROD_AHEAD + LOW_AHEAD)
            for n in range(FIRST):
                step(n)
            with dve.Fori(0, BODIES - 1) as T:
                for n in range(FIRST, FIRST + BODY):
                    step(n, T)
            for n in range(LAST, CHUNKS):
                step(n)
            for i in range(PIECES):
                sum_cur(GROUPS - 1, i)

            dve.wait_ge(top_in, 128)
            for m in (1, 3):
                dve.wait_ge(mlp_mm, 7 + m + 1)
                nc.vector.tensor_scalar(mlp1[1][m], (acc0, rep[:, 0, :])[m // 2][:, BANK:], bt1_sb[:, m:m + 1],
                                        0.0, ALU.add, ALU.max).then_inc(mlp_vec, 1)
            dve.wait_ge(mlp_mm, 13)
            nc.vector.tensor_scalar(mlp2[1][1], rep[:, 1, BANK:], bt2_sb[:, 1:2], 0.0, ALU.add, ALU.max)\
              .then_inc(mlp_vec, 1)

        @block.tensor
        def _(pe):
            def turn(k_tile, T=0, ds=range(DT)):
                if ds[0] == 0:
                    pe.wait_ge(parts_ready, k_tile // 2 + 1 + T)
                    if k_tile >= 2:
                        pe.wait_ge(hid_done, k_tile + 2 * T)
                for d in ds:
                    last = nc.tensor.transpose(turned_to(k_tile)[0:K0, d * P:(d + 1) * P],
                                               parts_b[:, (k_tile % 2) * DT + d, :, :], eye16_sb[:, :])
                if ds[-1] == DT - 1:
                    last.then_inc(parts_turned, 1)

            def copy(k_tile, T=0):
                if k_tile < 2:
                    pe.wait_ge(parts_kept, k_tile + 1)
                    src = x_parts[:, k_tile, :]
                else:
                    pe.wait_ge(next_kept, k_tile - 1 + 2 * T)
                    src = x_next[:, :]
                for h in range(0, TILE, BANK):
                    last = nc.tensor.matmul(copied_to(k_tile)[0:K0, h:h + BANK], sel0_sb[:, C0, 0:K0],
                                            src[:, h:h + BANK], start=True, stop=True)
                last.then_inc(copies_turned, 1)

            def repeat(n, T=0):
                k, layer, c, q = place(n)
                if layer == 0 and c == 0:
                    pe.wait_ge(parts_kept, k + 1 + 2 * T)
                if n == 1:
                    pe.wait_ge(parts_kept, 2)
                if n >= 2:
                    pe.wait_ge(prod_done, n - 1 + BODY * T)
                sel, half = (sel1_sb, (k - 1) % 2) if layer else (sel0_sb, k % 2)
                for h in range(0, TILE, BANK):
                    last = nc.tensor.matmul(rep[:, n % 2, h:h + BANK], sel[:, c, :],
                                            x_parts[:, half, h:h + BANK], start=True, stop=True)
                last.then_inc(rep_done, 1)

            def weigh(n, T=0):
                k, layer, c, q = place(n)
                rows, buf = rows_of(layer, c), n % NBUF
                if kind(n) == "-":
                    pe.wait_ge(prod_done, n + 1 + BODY * T)
                elif kind(n) == "v":
                    pe.wait_ge(low_v_done, through("v", n, T))
                else:
                    pe.wait_ge(low_p_done, through("p", n, T))
                if c == 0 and layer == 0:
                    pe.wait_ge(parts_kept, k + 1 + 2 * T)
                    pe.wait_ge(copies_kept, k + 1 + 2 * T)
                    if k >= 2:
                        pe.wait_ge(hid_done, k + 2 * T)
                if c == 0 and layer == 1:
                    pe.wait_ge(*((hid_done, 1) if k == 1 else (cur1_done, k - 1 + 2 * T)))
                acc = acc_of(k, layer)
                last_c = C1 - 1 if layer else C0 - 1
                if kind(n) == "-":
                    passes = [(w1_sb if layer else w0_sb, z, n % NZ, rows)]
                else:
                    high, low = (w1_high, w1_low) if layer else (w0_high, w0_low)
                    passes = [(high, z_high, buf, rows), (low, z_high, buf, rows), (high, z_low, buf, rows)]
                    if folded(layer, c):
                        passes = [(high, z_high, buf, rows), (low, z_high, buf, 2 * rows)]
                for i, (w, zz, at, rows) in enumerate(passes):
                    for h in range(0, TILE, BANK):
                        last = nc.tensor.matmul(acc[:, h:h + BANK], w[0:rows, c, :], zz[0:rows, at, h:h + BANK],
                                                start=(c == 0 and i == 0),
                                                stop=(c == last_c and i == len(passes) - 1))
                last.then_inc(main_done, 1)

            def mlp_first_half(at, q):
                out = acc0[:, (at % 2) * BANK:(at % 2 + 1) * BANK]
                if at == 0:
                    pe.wait_ge(top_in, 128)
                    pe.wait_ge(hid_done, TILES)
                    pe.wait_ge(direct_summed, GROUPS // 2)
                    pe.wait_ge(cur_summed, GROUPS // 2)
                if at >= 2:
                    pe.wait_ge(mlp_act, max(at - 1, 4 if at >= 4 else 0, 6 if at == 6 else 0))
                if at < 4:
                    nc.tensor.matmul(out, wt1_cur[:, at * P:(at + 1) * P], top_cur[:, 0:BANK],
                                     start=True, stop=False)
                    nc.tensor.matmul(out, wt1_dir[:, at * P:(at + 1) * P], top_dir[:, 0:BANK],
                                     start=False, stop=True).then_inc(mlp_mm, 1)
                elif at < 6:
                    m, second = at - 4, MULTIPLY_AT.get(q - 1) == [at]
                    for c in ((2, 3) if second else (0, 1)):
                        last = nc.tensor.matmul(out, wt2_sb[:, c, m * P:(m + 1) * P], mlp1[0][c],
                                                start=(c == 0), stop=(c == 3))
                    if second:
                        last.then_inc(mlp_mm, 1)
                else:
                    for c in range(2):
                        last = nc.tensor.matmul(acc0[0:1, 0:BANK], wt3_sb[:, c:c + 1], mlp2[0][c],
                                                start=(c == 0), stop=(c == 1))
                    last.then_inc(mlp_mm, 1)

            def step(n, T=0, ahead=REP_AHEAD):
                k, layer, c, q = place(n)
                weigh(n, T)
                if n + ahead < CHUNKS:
                    repeat(n + ahead, T)
                for at in MULTIPLY_AT.get(n - TAIL, ()):
                    mlp_first_half(at, n - TAIL)
                if 1 <= k < TILES - 1:
                    if 0 <= (q - Q_TURN) * TURN_EACH < DT:
                        turn(k + 1, T, range((q - Q_TURN) * TURN_EACH, (q - Q_TURN + 1) * TURN_EACH))
                    if q == Q_NEXT + 1:
                        copy(k + 1, T)

            pe.wait_ge(eye_in, 16)
            pe.wait_ge(sel_in, 32)
            turn(0)
            turn(1)
            copy(0)
            repeat(0)
            copy(1)
            for n in range(1, 3):
                repeat(n)
            pe.wait_ge(w_low_done, 4)
            ahead = 3
            for n in range(FIRST):
                step(n, ahead=ahead)
                if n % 2 and ahead < REP_AHEAD:
                    ahead += 1
                    repeat(n + ahead)
            with pe.Fori(0, BODIES - 1) as T:
                for n in range(FIRST, FIRST + BODY):
                    step(n, T)
            for n in range(LAST, CHUNKS):
                step(n)

            pe.wait_ge(direct_summed, GROUPS)
            pe.wait_ge(mlp_act, 7)
            out = [(acc0, rep[:, 0, :])[m // 2][:, (m % 2) * BANK:(m % 2 + 1) * BANK] for m in range(H1 // P)]
            for m in range(H1 // P):
                nc.tensor.matmul(out[m], wt1_dir[:, m * P:(m + 1) * P], top_dir[:, BANK:], start=True, stop=False)
            pe.wait_ge(cur_summed, GROUPS)
            for m in range(H1 // P):
                nc.tensor.matmul(out[m], wt1_cur[:, m * P:(m + 1) * P], top_cur[:, BANK:], start=False, stop=True)\
                  .then_inc(mlp_mm, 1)
            for m in range(H2 // P):
                for c in range(H1 // P):
                    if m == 0:
                        pe.wait_ge(*((mlp_vec, c // 2 + 1) if c % 2 else (mlp_act, 7 + c // 2 + 1)))
                    last = nc.tensor.matmul(rep[:, 1, m * BANK:(m + 1) * BANK], wt2_sb[:, c, m * P:(m + 1) * P],
                                            mlp1[1][c], start=(c == 0), stop=(c == H1 // P - 1))
                last.then_inc(mlp_mm, 1)
            for c in range(H2 // P):
                pe.wait_ge(*((mlp_vec, 3) if c else (mlp_act, 10)))
                last = nc.tensor.matmul(acc0[0:1, 0:BANK], wt3_sb[:, c:c + 1], mlp2[1][c],
                                        start=(c == 0), stop=(c == H2 // P - 1))
            last.then_inc(mlp_mm, 1)


def layout():
    shifts = list(range(1, SHIFTS - 1)) + [0, SHIFTS - 1]
    pair_a, pair_b = np.full((K0, C0), FIELDS * FIELDS), np.full((K0, C0), FIELDS * FIELDS)
    sel0, sel1 = np.zeros((3, FIELDS, C0 + 1, P)), np.zeros((3, FIELDS, C1, P))
    for at, s in enumerate(shifts):
        c, r = divmod(at, PER0)
        for j in range(FIELDS):
            i = (j + s) % FIELDS
            pair_a[r * FIELDS + j, c] = i * FIELDS + j
            if s:
                pair_b[r * FIELDS + j, c] = j * FIELDS + i
            sel0[:, i, c, r * FIELDS + j] = 1
    for r in range(PER0):
        for j in range(FIELDS):
            sel0[:, j, C0, r * FIELDS + j] = 1
    for i in range(FIELDS):
        sel1[:, i, i // 2, (i % 2) * HID:(i % 2 + 1) * HID] = 1
    return pair_a, pair_b, sel0.reshape(K0, C0 + 1, P), sel1.reshape(K0, C1, P)


def kernel(**inputs):
    import concourse.bacc as bacc
    import ml_dtypes
    from concourse.bass_utils import run_bass_kernel_spmd

    a = {k: np.asarray(v) for k, v in inputs.items()}
    pair_a, pair_b, sel0, sel1 = layout()
    w0 = np.concatenate([a["L0_rec_W0"], np.zeros((1, L), np.float32)])
    w1 = np.concatenate([a["L0_rec_W1"], a["L0_rec_W1"][FIELDS * HID - C1 * P:]])
    arrays = {
        "dense_t": a["dense_ctx"].T,
        "ids": a["ids"].reshape(GROUPS, P, FIELDS),
        **{f"tbl_{f}": a[f"tbl_{f}"] for f in range(FIELDS)},
        "w0_a": w0[pair_a], "w0_b": w0[pair_b],
        "w1": w1.reshape(C1, P, L).transpose(1, 0, 2),
        "sel0": sel0.astype(ml_dtypes.bfloat16), "sel1": sel1.astype(ml_dtypes.bfloat16),
        "eye16": np.eye(P, dtype=ml_dtypes.bfloat16),
        "wt1": a["W_top1"], "bt1": a["b_top1"].reshape(H1 // P, P).T,
        "wt2": a["W_top2"].reshape(H1 // P, P, H2).transpose(1, 0, 2), "bt2": a["b_top2"].reshape(H2 // P, P).T,
        "wt3": a["W_top3"].reshape(H2 // P, P).T,
    }
    arrays = {k: np.ascontiguousarray(v) for k, v in arrays.items()}
    nc = bacc.Bacc("TRN2", target_bir_lowering=False, num_devices=1)
    ap = {k: nc.dram_tensor(k, v.shape, mybir.dt.from_np(v.dtype), kind="ExternalInput").ap()
          for k, v in arrays.items()}
    y = nc.dram_tensor("y", (1, B), F32, kind="ExternalOutput").ap()
    tables = [ap.pop(f"tbl_{f}") for f in range(FIELDS)]
    program(nc, tables=tables, y=y, **ap)
    r = run_bass_kernel_spmd(nc, [arrays], core_ids=[0])
    return r.results[0]["y"].reshape(B, 1)
```
